# Optimizing a Trainium2 kernel written in Bass

```python
import numpy as np
import jax
import jax.numpy as jnp

def _softmax(x, axis=-1):
    return jax.nn.softmax(x, axis=axis)

def _gelu(x):
    return jax.nn.gelu(x, approximate=True)

def _silu(x):
    return jax.nn.silu(x)

def _sigmoid(x):
    return jax.nn.sigmoid(x)

def _layernorm(x, axis=-1, eps=1e-05):
    m = jnp.mean(x, axis=axis, keepdims=True)
    v = jnp.var(x, axis=axis, keepdims=True)
    return (x - m) / jnp.sqrt(v + eps)

def _scatter_add(tgt, idx, src, axis=0):
    return tgt.at[idx].add(src)

def _segment_sum(src, seg, n):
    return jax.ops.segment_sum(src, seg, n)
kernel_name = 'mk_adj_resnorm_d1_adj_r2_3fdbcf'

def setup_inputs(seed: int=0):
    np.random.seed(seed)
    _w = jnp.asarray

    def _rec_inputs():
        import jax
        import jax.numpy as jnp
        _gk = jax.random.key(seed)
        x = -0.000929 + 1 * jax.random.normal(jax.random.fold_in(_gk, 1), (8192, 128), jnp.float32)
        _a = jax.random.bernoulli(jax.random.fold_in(_gk, 2), 0.000976562, (8192, 8192))
        _a = jnp.logical_or(_a, jnp.eye(8192, dtype=bool))
        _af = _a.astype(jnp.float32)
        _af = _af * jax.random.uniform(jax.random.fold_in(_gk, 3), (8192, 8192), jnp.float32, 0.05, 1)
        adj = _af
        return (x, adj)
    x, adj = _rec_inputs()

    def _L0_gnn_setup():
        import jax, jax.numpy as jnp
        import numpy as np
        N = 4096
        D = 128
        key = jax.random.key(seed)
        kx, ka, kw1, kw2 = jax.random.split(key, 4)
        x = jax.random.normal(kx, (N, D), dtype=jnp.float32)
        A = jax.random.uniform(ka, (N, N), dtype=jnp.float32)
        s = 0.05
        W1 = jax.random.normal(kw1, (D, D), dtype=jnp.float32) * s
        b1 = jnp.zeros((D,), dtype=jnp.float32)
        W2 = jax.random.normal(kw2, (D, D), dtype=jnp.float32) * s
        b2 = jnp.zeros((D,), dtype=jnp.float32)
        return {'x': x, 'A': A, 'W1': W1, 'b1': b1, 'W2': W2, 'b2': b2}
    _L0_gnn_all = _L0_gnn_setup()
    _L0_gnn_in = {k: v for k, v in _L0_gnn_all.items() if k in ('W1', 'b1', 'W2', 'b2')}
    del _L0_gnn_all
    return {'x': x, 'adj': adj, 'L0_gnn_W1': _L0_gnn_in['W1'], 'L0_gnn_b1': _L0_gnn_in['b1'], 'L0_gnn_W2': _L0_gnn_in['W2'], 'L0_gnn_b2': _L0_gnn_in['b2']}

def reference(x, adj, L0_gnn_W1, L0_gnn_b1, L0_gnn_W2, L0_gnn_b2):
    import jax
    import jax.numpy as jnp

    def _L0_gnn_ref(x, A, W1, b1, W2, b2):
        import jax, jax.numpy as jnp
        import numpy as np
        N = 4096
        D = 128
        h = jax.nn.relu(jnp.matmul(A, jnp.matmul(x, W1)) + b1)
        h = jax.nn.relu(jnp.matmul(A, jnp.matmul(h, W2)) + b2)
        return h
    x = _layernorm(x + _L0_gnn_ref(x, adj, L0_gnn_W1, L0_gnn_b1, L0_gnn_W2, L0_gnn_b2), axis=-1)
    return x

_drawn_inputs = setup_inputs


def setup_inputs(seed=0):
    import zlib

    import numpy as np

    out = dict(_drawn_inputs(seed))
    spreads = {'L0_gnn_b1': (0.0, 0.1), 'L0_gnn_b2': (0.0, 0.1)}
    factors = {}
    for name, (base, spread) in spreads.items():
        noise = np.random.default_rng([zlib.crc32(name.encode()), seed]).standard_normal(out[name].shape)
        drawn = base * np.exp(spread * noise) if base else spread * noise
        out[name] = jnp.asarray(drawn.astype(out[name].dtype))
    for name, factor in factors.items():
        out[name] = (out[name] * factor).astype(out[name].dtype)
    return out
```

```python
from contextlib import ExitStack

import concourse.bass as bass
from concourse import mybir

ALU = mybir.AluOpType
ACT = mybir.ActivationFunctionType
F32 = mybir.dt.float32
F32R = mybir.dt.float32r

P = 128
D = 128
BLOCK = 512
TILES = BLOCK // P
HALF = 2
CHUNKS = TILES // HALF
RING = 4
GROUP = 4
EPS = 1e-5

LAYER1, FUSED, AGAIN = "layer1", "fused", "again"


def row_plan(phase, blocks):
    known = GROUP * phase
    single = [(LAYER1, None, kb) for kb in range(known, blocks)]
    again = [(AGAIN, q, kb) for q in range(phase) for kb in range(known - GROUP, known)]
    fused = [(FUSED, None, kb) for kb in range(known)]
    light = single[:1] + again + single[1:-3]
    plan, used = [], 0
    for n, block in enumerate(light):
        plan.append(block)
        while used < len(fused) * (n + 1) // len(light):
            plan.append(fused[used])
            used += 1
    return plan + single[-3:]


class Row:

    def __init__(self, phase, blocks):
        self.phase = phase
        self.plan = row_plan(phase, blocks)
        self.chunks = [(kind, q, kb, half) for kind, q, kb in self.plan for half in range(CHUNKS)]
        self.first, self.last = {}, {}
        for n, (kind, q, _, _) in enumerate(self.chunks):
            sums = {LAYER1: ["one"], FUSED: ["one", "two"], AGAIN: [q]}[kind]
            for s in sums:
                self.first.setdefault(s, n)
                self.last[s] = n
        self.leaving = sorted((s for s in self.last if s != "one"), key=lambda s: self.last[s])

    def leaving_before(self, n):
        return [s for s in self.leaving if self.last[s] + RING == n]


def gnn_kernel(nc, a_t, x_t, w1, b1, w2, b2, ident, out):
    blocks = x_t.shape[1] // BLOCK
    phases = blocks // GROUP
    rows = [Row(p, blocks) for p in range(phases)]
    per_row = [len(r.chunks) for r in rows]
    in_dram = blocks * CHUNKS
    begins = [GROUP * sum(per_row[:p]) for p in range(phases + 1)]
    leaves = [GROUP * sum(len(r.leaving) for r in rows[:p]) for p in range(phases + 1)]
    closing = [(kb, half) for kb in range(blocks - GROUP, blocks) for half in range(CHUNKS)]
    assert all(n % RING == 0 for n in per_row) and len(closing) == 8 and blocks % 2 == 0

    with ExitStack() as ctx:
        def sb(name, shape, dt=F32):
            return ctx.enter_context(nc.sbuf_tensor(name, shape, dt))

        def psum(name, shape):
            return ctx.enter_context(nc.psum_tensor(name, shape, F32))

        def sem(name):
            return ctx.enter_context(nc.semaphore(name))

        y_hi = sb("y_hi", [P, blocks, BLOCK], F32R)
        y_lo = sb("y_lo", [P, blocks, BLOCK], F32R)
        z_hi = sb("z_hi", [P, blocks, BLOCK], F32R)
        z_lo = sb("z_lo", [P, blocks, BLOCK], F32R)
        a_raw = sb("a_raw", [P, RING, HALF * BLOCK])
        a_hi = sb("a_hi", [P, RING, HALF * BLOCK], F32R)
        a_lo = sb("a_lo", [P, RING, HALF * BLOCK], F32R)
        side = sb("side", [P, blocks, BLOCK])
        row_t = sb("row_t", [P, BLOCK])
        x_again = sb("x_again", [P, BLOCK])
        result = sb("result", [P, 2, BLOCK])
        w1_sb = sb("w1_sb", [P, D])
        w2_sb = sb("w2_sb", [P, D])
        id_sb = sb("id_sb", [P, P])
        bias = sb("bias", [P, 2])
        stats = sb("stats", [P, TILES, 6])
        mean_var = sb("mean_var", [P, TILES, 2])
        eps = sb("eps", [P, 1])
        deviation = sb("deviation", [P, TILES])
        inverse = sb("inverse", [P, TILES])
        shift = sb("shift", [P, TILES])

        one = psum("one", [P, 2, BLOCK])
        two = psum("two", [P, BLOCK])
        again = psum("again", [P, 2, BLOCK])
        small = psum("small", [P, 2, BLOCK])

        w1_in, weights_in, eps_set = sem("w1_in"), sem("weights_in"), sem("eps_set")
        x_in = [sem(f"x_in{g}") for g in range(phases)]
        a_in = [sem(f"a_in{s}") for s in range(RING)]
        a_hi_made = sem("a_hi_made")
        a_lo_made = sem("a_lo_made")
        a_used = sem("a_used")
        y_summed, y_hi_made, y_lo_made = sem("y_summed"), sem("y_hi_made"), sem("y_lo_made")
        h1_made = sem("h1_made")
        z_summed, z_hi_made, z_lo_made = sem("z_summed"), sem("z_hi_made"), sem("z_lo_made")
        two_left = sem("two_left")
        h2_summed, h2_made, x_again_in = sem("h2_summed"), sem("h2_made"), sem("x_again_in")
        residual_made, turned, measured = sem("residual_made"), sem("turned"), sem("measured")
        variance_made, rooted, inverted = sem("variance_made"), sem("rooted"), sem("inverted")
        shift_made, result_made = sem("shift_made"), sem("result_made")
        stored = [sem(f"stored{s}") for s in range(2)]

        def turns(eng, turn):
            for p, row in enumerate(rows):
                if p == 0:
                    turn(row, 0, 0, False)
                with eng.Fori(0 if p else 1, GROUP) as j:
                    turn(row, j * per_row[p] + begins[p], j + GROUP * p, True)

        def windows(eng, window):
            def at(w):
                window(w, w % 2, lambda lag: 0 <= w - lag < blocks)

            for w in range(4):
                at(w)
            with eng.Fori(2, blocks // 2) as i:
                for parity in range(2):
                    window(i * 2 + parity, parity, lambda lag: True)
            for w in range(blocks, blocks + 4):
                at(w)

        def closing_base(w):
            return w * len(closing) + begins[phases]

        block = ctx.enter_context(nc.Block())

        @block.sync
        def _(sp):
            def load(n, base, chunk, first=False):
                if not first:
                    sp.wait_ge(a_lo_made, base + (n - RING + 1))
                sp.dma_start(a_raw[:, n % RING, :], a_t[chunk, :, :]).then_inc(a_in[n % RING], 16)

            def load_x(g):
                sp.dma_start(side[:, GROUP * g:GROUP * (g + 1), :],
                             x_t[:, GROUP * g * BLOCK:GROUP * (g + 1) * BLOCK]
                             .rearrange("p (b i) -> p b i", i=BLOCK)).then_inc(x_in[g], 16)

            def turn(row, base, r, later):
                if not later:
                    sp.dma_start(w1_sb[:, :], w1).then_inc(w1_in, 16)
                    load_x(0)
                for n, (kind, q, kb, half) in enumerate(row.chunks):
                    of = r - GROUP * (row.phase - q) if kind == AGAIN else r
                    load(n, base, of * in_dram + (CHUNKS * kb + half), not later and n < RING)
                    if not later and n == 0:
                        sp.dma_start(w2_sb[:, :], w2).then_inc(weights_in, 16)
                        sp.dma_start(bias[:, 0:1], b1).then_inc(weights_in, 16)
                        sp.dma_start(bias[:, 1:2], b2).then_inc(weights_in, 16)
                        sp.dma_start(id_sb[:, :], ident).then_inc(weights_in, 16)
                    if not later and n % 4 == 2 and n // 4 + 1 < phases:
                        load_x(n // 4 + 1)

            turns(sp, turn)

            def window(w, parity, has):
                for n, (kb, half) in enumerate(closing):
                    if has(0):
                        load(n, closing_base(w), w * in_dram + (CHUNKS * kb + half))
                    if n == 6 and has(3):
                        sp.wait_ge(result_made, w - 2)
                        sp.dma_start(out[w - 3, :, :], result[:, 1 - parity, :]).then_inc(stored[1 - parity], 16)
                    if n == 7 and has(1):
                        if has(2):
                            sp.wait_ge(residual_made, w - 1)
                        sp.dma_start(x_again[:, :], x_t[:, bass.ds((w - 1) * BLOCK, BLOCK)]).then_inc(x_again_in, 16)

            windows(sp, window)
            for parity in range(2):
                sp.wait_ge(stored[parity], 16 * (blocks // 2))

        @block.scalar
        def _(act):
            def round_chunk(n, base, first=False):
                act.wait_ge(a_in[n % RING], base * (16 // RING) + 16 * (n // RING + 1))
                if not first:
                    act.wait_ge(a_used, base + (n - RING + 1))
                nc.scalar.copy(a_hi[:, n % RING, :], a_raw[:, n % RING, :]).then_inc(a_hi_made, 1)

            def round_y(kb):
                act.wait_ge(y_summed, kb + 1)
                nc.scalar.copy(y_hi[:, kb, :], small[:, kb % 2, :]).then_inc(y_hi_made, 1)

            def round_z(r):
                act.wait_ge(z_summed, r + 1)
                nc.scalar.copy(z_hi[:, bass.ds(r, 1), :], small[:, 0:1, :]).then_inc(z_hi_made, 1)

            nc.scalar.preload_act_table(ACT.Sqrt)

            def turn(row, base, r, later):
                for n in range(len(row.chunks)):
                    if later and n == 6:
                        round_z(r - 1)
                    if not later and n < 2:
                        round_y(n)
                    if not later and n >= 5 and n % 2 == 1:
                        round_y(n // 2)
                    round_chunk(n, base, not later and n < RING)

            turns(act, turn)

            def window(w, parity, has):
                for n in range(len(closing)):
                    if n == 5 and has(0) and not has(1):
                        round_z(blocks - 1)
                    if n == 3 and has(2):
                        if not has(3):
                            act.wait_ge(eps_set, 1)
                        act.wait_ge(variance_made, w - 1)
                        nc.scalar.activation(deviation[:, :], mean_var[:, :, 1], ACT.Sqrt, bias=eps[:, 0:1])\
                            .then_inc(rooted, 1)
                    if n == 5 and has(1):
                        act.wait_ge(h2_summed, w)
                        h2_t = side[:, bass.ds(w - 1, 1), :]
                        nc.scalar.activation(h2_t, h2_t, ACT.Relu, bias=bias[:, 1:2]).then_inc(h2_made, 1)
                    if n == 7 and has(2):
                        act.wait_ge(shift_made, w - 1)
                        if has(4):
                            act.wait_ge(stored[parity], w * 8 - (16 + 8 * parity))
                        for t in range(TILES):
                            cols = slice(t * D, (t + 1) * D)
                            scaled = nc.scalar.activation(result[:, parity, cols], one[:, parity, cols], ACT.Identity,
                                                          scale=inverse[:, t:t + 1], bias=shift[:, t:t + 1])
                        scaled.then_inc(result_made, 1)
                    if has(0):
                        round_chunk(n, closing_base(w))

            windows(act, window)

        @block.vector
        def _(dve):
            def rest_of_chunk(n, base):
                dve.wait_ge(a_hi_made, base + (n + 1))
                nc.vector.tensor_tensor(a_lo[:, n % RING, :], a_raw[:, n % RING, :], a_hi[:, n % RING, :],
                                        ALU.subtract).then_inc(a_lo_made, 1)

            def rest_of_y(kb):
                dve.wait_ge(y_hi_made, kb + 1)
                nc.vector.tensor_tensor(y_lo[:, kb, :], small[:, kb % 2, :], y_hi[:, kb, :],
                                        ALU.subtract).then_inc(y_lo_made, 1)

            def rest_of_z(r):
                dve.wait_ge(z_hi_made, r + 1)
                nc.vector.tensor_tensor(z_lo[:, bass.ds(r, 1), :], small[:, 0:1, :], z_hi[:, bass.ds(r, 1), :],
                                        ALU.subtract).then_inc(z_lo_made, 1)

            def make_h1(r, chunks, parity):
                dve.wait_ge(weights_in, 64)
                dve.wait_ge(a_used, chunks)
                nc.vector.tensor_scalar(row_t[:, :], one[:, parity, :], bias[:, 0:1], 0.0, ALU.add, ALU.max)\
                    .then_inc(h1_made, 1)

            def take_out(s, row, base, r):
                dve.wait_ge(a_used, base + (row.last[s] + 1))
                of = r if s == "two" else r - GROUP * (row.phase - s)
                total = side[:, bass.ds(of, 1), :]
                part = two[:, None, :] if s == "two" else again[:, s % 2:s % 2 + 1, :]
                if s == "two" or (s == 0 and row.phase == 1):
                    nc.vector.tensor_copy(total, part).then_inc(two_left, 1)
                else:
                    nc.vector.tensor_tensor(total, part, total, ALU.add).then_inc(two_left, 1)

            nc.vector.memset(eps[:, :], EPS).then_inc(eps_set, 1)
            dve.wait_ge(eps_set, 1)
            nc.vector.memset(shift[:, :], 0.0).then_inc(two_left, 1)

            def turn(row, base, r, later):
                for n in range(len(row.chunks)):
                    if later and n == 3:
                        make_h1(r - 1, base, bass.ds((r - 1) % 2, 1))
                    if later and n == 6:
                        rest_of_z(r - 1)
                    if not later and n < 2:
                        rest_of_y(n)
                    if not later and n >= 5 and n % 2 == 1:
                        rest_of_y(n // 2)
                    for s in row.leaving_before(n):
                        take_out(s, row, base, r)
                    rest_of_chunk(n, base)

            turns(dve, turn)

            def window(w, parity, has):
                for n in range(len(closing)):
                    if n == 3 and has(0) and not has(1):
                        make_h1(blocks - 1, begins[phases], slice((blocks - 1) % 2, (blocks - 1) % 2 + 1))
                    if n == 5 and has(0) and not has(1):
                        rest_of_z(blocks - 1)
                    if n == 1 and has(2):
                        dve.wait_ge(turned, w - 1)
                        for t in range(TILES):
                            last = nc.vector.bn_stats(stats[:, t, :], one[:, parity, t * D:(t + 1) * D])
                        last.then_inc(measured, 1)
                        dve.wait_ge(measured, w - 1)
                    if n == 3 and has(1):
                        dve.wait_ge(a_used, closing_base(w))
                        total = side[:, bass.ds(w - 1, 1), :]
                        nc.vector.tensor_tensor(total, again[:, 1 - parity:2 - parity, :], total, ALU.add)\
                            .then_inc(h2_summed, 1)
                    if n == 5 and has(2):
                        dve.wait_ge(rooted, w - 1)
                        if has(3):
                            dve.wait_ge(result_made, w - 2)
                        nc.vector.reciprocal(inverse[:, :], deviation[:, :]).then_inc(inverted, 1)
                        dve.wait_ge(inverted, w - 1)
                        nc.vector.scalar_tensor_tensor(out=shift[:, :], in0=mean_var[:, :, 0], scalar=-1.0,
                                                       in1=inverse[:, :], op0=ALU.mult, op1=ALU.mult)\
                            .then_inc(shift_made, 1)
                    if has(0):
                        rest_of_chunk(n, closing_base(w))
                    if n == 1 and has(2):
                        for t in range(TILES):
                            last = nc.vector.bn_aggr(mean_var[:, t, :], stats[:, t, :])
                        last.then_inc(variance_made, 1)

            windows(dve, window)

        @block.gpsimd
        def _(pool):
            pool.wait_ge(z_summed, blocks)
            pool.wait_ge(weights_in, 64)

            def add_x(r, first=False):
                if not first:
                    pool.wait_ge(turned, r)
                pool.wait_ge(h2_made, r + 1)
                pool.wait_ge(x_again_in, r * 16 + 16)
                nc.gpsimd.tensor_tensor(row_t[:, None, :], side[:, bass.ds(r, 1), :], x_again[:, None, :], ALU.add)\
                    .then_inc(residual_made, 1)

            add_x(0, True)
            with pool.Fori(1, blocks) as r:
                add_x(r)

        @block.tensor
        def _(pe):
            def sum_chunk(n, base, targets, half, kb):
                slot = n % RING
                pe.wait_ge(a_lo_made, base + (n + 1))
                for t in range(HALF):
                    k = (HALF * half + t) * P
                    i = slice(t * BLOCK, (t + 1) * BLOCK)
                    for total, hi, lo, begins_here, ends_here in targets:
                        nc.tensor.matmul(total, lo[:, kb, k:k + P], a_hi[:, slot, i],
                                         start=begins_here and t == 0, stop=False)
                        nc.tensor.matmul(total, hi[:, kb, k:k + P], a_hi[:, slot, i], start=False, stop=False)
                        last = nc.tensor.matmul(total, hi[:, kb, k:k + P], a_lo[:, slot, i], start=False,
                                                stop=ends_here and t == HALF - 1)
                last.then_inc(a_used, 1)

            def sum_y(kb):
                if kb % GROUP == 0:
                    pe.wait_ge(x_in[kb // GROUP], 16)
                for t in range(TILES):
                    last = nc.tensor.matmul(small[:, kb % 2, t * D:(t + 1) * D], side[:, kb, t * P:(t + 1) * P],
                                            w1_sb[:, :], start=True, stop=True)
                last.then_inc(y_summed, 1)

            def sum_z(r):
                pe.wait_ge(weights_in, 64)
                pe.wait_ge(h1_made, r + 1)
                for t in range(TILES):
                    last = nc.tensor.matmul(small[:, 0, t * D:(t + 1) * D], row_t[:, t * P:(t + 1) * P],
                                            w2_sb[:, :], start=True, stop=True)
                last.then_inc(z_summed, 1)

            def turn(row, base, r, later):
                if not later:
                    pe.wait_ge(w1_in, 16)
                    sum_y(0)
                    sum_y(1)
                left = (r - GROUP * row.phase) * len(row.leaving) + (leaves[row.phase] + 1)
                parity = pe.snap(r % 2) if later else 0
                for n, (kind, q, kb, half) in enumerate(row.chunks):
                    targets = []
                    if kind in (LAYER1, FUSED):
                        if not later and half == 0:
                            pe.wait_ge(y_lo_made, kb + 1)
                        targets.append((one[:, bass.ds(parity, 1), :] if later else one[:, 0, :], y_hi, y_lo,
                                        n == row.first["one"], n == row.last["one"]))
                    if kind == FUSED:
                        if n == row.first["two"]:
                            pe.wait_ge(two_left, left)
                        targets.append((two[:, :], z_hi, z_lo, n == row.first["two"], n == row.last["two"]))
                    if kind == AGAIN:
                        if n == row.first[q]:
                            pe.wait_ge(two_left, left + (row.leaving.index(q - 2) + 1 if q >= 2 else 0))
                        targets.append((again[:, q % 2, :], z_hi, z_lo, n == row.first[q], n == row.last[q]))
                    if kind in (FUSED, AGAIN) and half == 0:
                        pe.wait_ge(z_lo_made, kb + 1)
                    sum_chunk(n, base, targets, half, kb)
                    if later and n == 1:
                        sum_z(r - 1)
                    if not later and half == CHUNKS - 1 and kb + 2 < blocks:
                        sum_y(kb + 2)

            turns(pe, turn)

            def window(w, parity, has):
                for n, (kb, half) in enumerate(closing):
                    if has(0):
                        if n == 0 and has(2):
                            pe.wait_ge(h2_summed, w - 1)
                        elif n == 0:
                            pe.wait_ge(two_left, leaves[phases] + 1)
                        if n == 6 and not has(1):
                            pe.wait_ge(z_lo_made, blocks)
                        sum_chunk(n, closing_base(w), [(again[:, parity, :], z_hi, z_lo, n == 0, n == 7)], half, kb)
                        if n == 1 and not has(1):
                            sum_z(blocks - 1)
                    if n == 5 and has(1):
                        pe.wait_ge(residual_made, w)
                        if has(3):
                            pe.wait_ge(result_made, w - 2)
                        for t in range(TILES):
                            last = nc.tensor.transpose(one[:, 1 - parity, t * D:(t + 1) * D],
                                                       row_t[:, t * P:(t + 1) * P], id_sb[:, :])
                        last.then_inc(turned, 1)

            windows(pe, window)


def kernel(x, adj, L0_gnn_W1, L0_gnn_b1, L0_gnn_W2, L0_gnn_b2):
    import numpy as np

    import concourse.bacc as bacc
    from concourse.bass_utils import run_bass_kernel_spmd

    n = adj.shape[0]
    blocks = n // BLOCK
    a_t = np.asarray(adj).reshape(blocks, BLOCK, blocks, CHUNKS, HALF, P).transpose(0, 2, 3, 5, 4, 1)
    arrays = {
        "a_t": np.ascontiguousarray(a_t).reshape(blocks * blocks * CHUNKS, P, HALF * BLOCK),
        "x_t": np.ascontiguousarray(np.asarray(x).T),
        "w1": np.asarray(L0_gnn_W1),
        "b1": np.asarray(L0_gnn_b1).reshape(D, 1),
        "w2": np.asarray(L0_gnn_W2),
        "b2": np.asarray(L0_gnn_b2).reshape(D, 1),
        "ident": np.eye(P, dtype=np.float32),
    }
    nc = bacc.Bacc("TRN2", target_bir_lowering=False, num_devices=1, dynamic_dma_scratch_size=4096)
    ins = [nc.dram_tensor(name, a.shape, F32, kind="ExternalInput").ap() for name, a in arrays.items()]
    out = nc.dram_tensor("out", (blocks, P, BLOCK), F32, kind="ExternalOutput").ap()
    gnn_kernel(nc, *ins, out)
    result = run_bass_kernel_spmd(nc, [arrays], core_ids=[0]).results[0]["out"]
    return np.asarray(result).reshape(blocks, P, TILES, D).transpose(0, 2, 1, 3).reshape(n, D)
```

```python
from contextlib import ExitStack

import concourse.bass as bass
from concourse import mybir

ALU = mybir.AluOpType
ACT = mybir.ActivationFunctionType
F32 = mybir.dt.float32
F32R = mybir.dt.float32r

P = 128
D = 128
BLOCK = 512
TILES = BLOCK // P
HALF = 2
CHUNKS = TILES // HALF
RING = 4
GROUPS = (2, 2, 4, 4, 2, 2)
X_GROUP = 4
LAGS = 6
EPS = 1e-5

LAYER1, FUSED, AGAIN = "layer1", "fused", "again"


def row_plan(phase):
    known, blocks = sum(GROUPS[:phase]), sum(GROUPS)
    single = [(LAYER1, None, kb) for kb in range(known, blocks)]
    again = [(AGAIN, q, kb) for q in range(known // GROUPS[phase]) for kb in range(known - GROUPS[phase - 1], known)]
    fused = [(FUSED, None, kb) for kb in range(known)]
    begin = single[:-2][:2]
    light = begin + again + single[len(begin):-2]
    plan, used = [], 0
    for n, block in enumerate(light):
        plan.append(block)
        while used < len(fused) * (n + 1) // len(light):
            plan.append(fused[used])
            used += 1
    return plan + single[-2:]


class Row:

    def __init__(self, phase):
        self.phase, self.group, self.start = phase, GROUPS[phase], sum(GROUPS[:phase])
        self.chunks = [(kind, q, kb, half) for kind, q, kb in row_plan(phase) for half in range(CHUNKS)]
        self.first, self.last = {}, {}
        for n, (kind, q, _, _) in enumerate(self.chunks):
            sums = {LAYER1: ["one"], FUSED: ["one", "two"], AGAIN: [q]}[kind]
            for s in sums:
                self.first.setdefault(s, n)
                self.last[s] = n
        self.leaving = sorted((s for s in self.last if s != "one"), key=lambda s: self.last[s])
        assert all(self.last[s] + RING < len(self.chunks) for s in self.leaving) and len(self.chunks) % RING == 0

    def leaving_before(self, n):
        return [s for s in self.leaving if self.last[s] + RING == n]

    def row_of(self, q, r):
        return r + (self.group * q - self.start)


def gnn_kernel(nc, a_t, x_t, w1, b1, w2, b2, ident, out):
    blocks = x_t.shape[1] // BLOCK
    assert blocks == sum(GROUPS)
    phases = len(GROUPS)
    rows = [Row(p) for p in range(phases)]
    per_row = [len(r.chunks) for r in rows]
    in_dram = blocks * CHUNKS
    begins = [sum(r.group * len(r.chunks) for r in rows[:p]) for p in range(phases + 1)]
    leaves = [sum(r.group * len(r.leaving) for r in rows[:p]) for p in range(phases + 1)]
    closing = [(kb, half) for kb in range(blocks - GROUPS[-1], blocks) for half in range(CHUNKS)]
    assert len(closing) == RING and blocks % 2 == 0

    with ExitStack() as ctx:
        def sb(name, shape, dt=F32):
            return ctx.enter_context(nc.sbuf_tensor(name, shape, dt))

        def psum(name, shape):
            return ctx.enter_context(nc.psum_tensor(name, shape, F32))

        def sem(name):
            return ctx.enter_context(nc.semaphore(name))

        y_hi = sb("y_hi", [P, blocks, BLOCK], F32R)
        y_lo = sb("y_lo", [P, blocks, BLOCK], F32R)
        z_hi = sb("z_hi", [P, blocks, BLOCK], F32R)
        z_lo = sb("z_lo", [P, blocks, BLOCK], F32R)
        a_raw = sb("a_raw", [P, RING, HALF * BLOCK])
        a_hi = sb("a_hi", [P, RING, HALF * BLOCK], F32R)
        a_lo = sb("a_lo", [P, RING, HALF * BLOCK], F32R)
        side = sb("side", [P, blocks, BLOCK])
        row_t = sb("row_t", [P, BLOCK])
        x_again = sb("x_again", [P, 2, BLOCK])
        result = sb("result", [P, 2, BLOCK])
        w1_sb = sb("w1_sb", [P, D])
        w2_sb = sb("w2_sb", [P, D])
        id_sb = sb("id_sb", [P, P])
        bias = sb("bias", [P, 2])
        stats = sb("stats", [P, TILES, 6])
        mean_var = sb("mean_var", [P, TILES, 2])
        eps = sb("eps", [P, 1])
        deviation = sb("deviation", [P, TILES])
        inverse = sb("inverse", [P, TILES])
        shift = sb("shift", [P, TILES])

        one = psum("one", [P, 2, BLOCK])
        two = psum("two", [P, BLOCK])
        again = psum("again", [P, 2, BLOCK])
        small = psum("small", [P, 2, BLOCK])

        w1_in, weights_in, eps_set = sem("w1_in"), sem("weights_in"), sem("eps_set")
        x_in = [sem(f"x_in{g}") for g in range(blocks // X_GROUP)]
        a_in = [sem(f"a_in{s}") for s in range(RING)]
        a_hi_made = sem("a_hi_made")
        a_lo_made = sem("a_lo_made")
        a_used = sem("a_used")
        y_summed, y_hi_made, y_lo_made = sem("y_summed"), sem("y_hi_made"), sem("y_lo_made")
        h1_made = sem("h1_made")
        z_summed, z_hi_made, z_lo_made = sem("z_summed"), sem("z_hi_made"), sem("z_lo_made")
        two_left = sem("two_left")
        h2_summed, h2_made = sem("h2_summed"), sem("h2_made")
        x_again_in = [sem(f"x_again_in{s}") for s in range(2)]
        residual_made, turned, measured = sem("residual_made"), sem("turned"), sem("measured")
        variance_made, rooted, inverted = sem("variance_made"), sem("rooted"), sem("inverted")
        shift_made, result_made = sem("shift_made"), sem("result_made")
        stored = [sem(f"stored{s}") for s in range(2)]

        def turns(eng, turn):
            for p, row in enumerate(rows):
                if p == 0:
                    for j in range(row.group):
                        turn(row, j * per_row[p], j, j > 0)
                    continue
                with eng.Fori(0, row.group) as j:
                    turn(row, j * per_row[p] + begins[p], j + row.start, True)

        def windows(eng, window):
            def at(w):
                window(w, w % 2, lambda lag: 0 <= w - lag < blocks)

            for w in range(LAGS):
                at(w)
            with eng.Fori(LAGS // 2, blocks // 2) as i:
                for parity in range(2):
                    window(i * 2 + parity, parity, lambda lag: True)
            for w in range(blocks, blocks + LAGS):
                at(w)

        def closing_base(w):
            return w * len(closing) + begins[phases]

        block = ctx.enter_context(nc.Block())

        @block.sync
        def _(sp):
            def load(n, base, chunk, first=False):
                if not first:
                    sp.wait_ge(a_lo_made, base + (n - RING + 1))
                sp.dma_start(a_raw[:, n % RING, :], a_t[chunk, :, :]).then_inc(a_in[n % RING], 16)

            def load_x(g):
                sp.dma_start(side[:, X_GROUP * g:X_GROUP * (g + 1), :],
                             x_t[:, X_GROUP * g * BLOCK:X_GROUP * (g + 1) * BLOCK]
                             .rearrange("p (b i) -> p b i", i=BLOCK)).then_inc(x_in[g], 16)

            def turn(row, base, r, later):
                if not later:
                    sp.dma_start(w1_sb[:, :], w1).then_inc(w1_in, 16)
                    load_x(0)
                for n, (kind, q, kb, half) in enumerate(row.chunks):
                    of = row.row_of(q, r) if kind == AGAIN else r
                    load(n, base, of * in_dram + (CHUNKS * kb + half), not later and n < RING)
                    if not later and n == 0:
                        sp.dma_start(w2_sb[:, :], w2).then_inc(weights_in, 16)
                        sp.dma_start(bias[:, 0:1], b1).then_inc(weights_in, 16)
                        sp.dma_start(bias[:, 1:2], b2).then_inc(weights_in, 16)
                        sp.dma_start(id_sb[:, :], ident).then_inc(weights_in, 16)
                    if not later and n % 4 == 2 and n // 4 + 1 < len(x_in):
                        load_x(n // 4 + 1)

            turns(sp, turn)

            def window(w, parity, has):
                for n, (kb, half) in enumerate(closing):
                    if has(0):
                        load(n, closing_base(w), w * in_dram + (CHUNKS * kb + half))
                    if n == 3 and has(5):
                        sp.wait_ge(result_made, w - 4)
                        sp.dma_start(out[w - 5, :, :], result[:, 1 - parity, :]).then_inc(stored[1 - parity], 16)
                    if n == 3 and has(2):
                        if has(4):
                            sp.wait_ge(residual_made, w - 3)
                        sp.dma_start(x_again[:, parity, :], x_t[:, bass.ds((w - 2) * BLOCK, BLOCK)])\
                            .then_inc(x_again_in[parity], 16)

            windows(sp, window)
            for parity in range(2):
                sp.wait_ge(stored[parity], 16 * (blocks // 2))

        @block.scalar
        def _(act):
            def round_chunk(n, base, first=False):
                act.wait_ge(a_in[n % RING], base * (16 // RING) + 16 * (n // RING + 1))
                if not first:
                    act.wait_ge(a_used, base + (n - RING + 1))
                nc.scalar.copy(a_hi[:, n % RING, :], a_raw[:, n % RING, :]).then_inc(a_hi_made, 1)

            def round_y(kb):
                act.wait_ge(y_summed, kb + 1)
                nc.scalar.copy(y_hi[:, kb, :], small[:, kb % 2, :]).then_inc(y_hi_made, 1)

            def round_z(r):
                act.wait_ge(z_summed, r + 1)
                nc.scalar.copy(z_hi[:, bass.ds(r, 1), :], small[:, 0:1, :]).then_inc(z_hi_made, 1)

            nc.scalar.preload_act_table(ACT.Sqrt)

            def turn(row, base, r, later):
                for n in range(len(row.chunks)):
                    if later and n == 6:
                        round_z(r - 1)
                    if not later and n < 2:
                        round_y(n)
                    if not later and n >= 5 and n % 2 == 1:
                        round_y(n // 2)
                    round_chunk(n, base, not later and n < RING)

            turns(act, turn)

            def window(w, parity, has):
                for n in range(len(closing)):
                    if n == 0 and has(1) and not has(2):
                        round_z(blocks - 1)
                    if n == 1 and has(2):
                        act.wait_ge(h2_summed, w - 1)
                        h2_t = side[:, bass.ds(w - 2, 1), :]
                        nc.scalar.activation(h2_t, h2_t, ACT.Relu, bias=bias[:, 1:2]).then_inc(h2_made, 1)
                    if n == 2 and has(4):
                        act.wait_ge(shift_made, w - 3)
                        if has(6):
                            act.wait_ge(stored[parity], w * 8 - (32 + 8 * parity))
                    if n >= 2 and has(4):
                        for t in range(TILES // 2 * (n - 2), TILES // 2 * (n - 1)):
                            cols = slice(t * D, (t + 1) * D)
                            scaled = nc.scalar.activation(result[:, parity, cols], one[:, parity, cols], ACT.Identity,
                                                          scale=inverse[:, t:t + 1], bias=shift[:, t:t + 1])
                        if n == 3:
                            scaled.then_inc(result_made, 1)
                    if n == 3 and has(3):
                        if not has(4):
                            act.wait_ge(eps_set, 1)
                        act.wait_ge(variance_made, w - 2)
                        nc.scalar.activation(deviation[:, :], mean_var[:, :, 1], ACT.Sqrt, bias=eps[:, 0:1])\
                            .then_inc(rooted, 1)
                    if has(0):
                        round_chunk(n, closing_base(w))

            windows(act, window)

        @block.vector
        def _(dve):
            def rest_of_chunk(n, base):
                dve.wait_ge(a_hi_made, base + (n + 1))
                nc.vector.tensor_tensor(a_lo[:, n % RING, :], a_raw[:, n % RING, :], a_hi[:, n % RING, :],
                                        ALU.subtract).then_inc(a_lo_made, 1)

            def rest_of_y(kb):
                dve.wait_ge(y_hi_made, kb + 1)
                nc.vector.tensor_tensor(y_lo[:, kb, :], small[:, kb % 2, :], y_hi[:, kb, :],
                                        ALU.subtract).then_inc(y_lo_made, 1)

            def rest_of_z(r):
                dve.wait_ge(z_hi_made, r + 1)
                nc.vector.tensor_tensor(z_lo[:, bass.ds(r, 1), :], small[:, 0:1, :], z_hi[:, bass.ds(r, 1), :],
                                        ALU.subtract).then_inc(z_lo_made, 1)

            def make_h1(r, chunks, parity):
                dve.wait_ge(weights_in, 64)
                dve.wait_ge(a_used, chunks)
                nc.vector.tensor_scalar(row_t[:, :], one[:, parity, :], bias[:, 0:1], 0.0, ALU.add, ALU.max)\
                    .then_inc(h1_made, 1)

            def take_out(s, row, base, r):
                dve.wait_ge(a_used, base + (row.last[s] + 1))
                of = r if s == "two" else row.row_of(s, r)
                total = side[:, bass.ds(of, 1), :]
                part = two[:, None, :] if s == "two" else again[:, s % 2:s % 2 + 1, :]
                if s == "two" or row.phase == 1:
                    nc.vector.tensor_copy(total, part).then_inc(two_left, 1)
                else:
                    nc.vector.tensor_tensor(total, part, total, ALU.add).then_inc(two_left, 1)

            nc.vector.memset(eps[:, :], EPS).then_inc(eps_set, 1)
            dve.wait_ge(eps_set, 1)
            nc.vector.memset(shift[:, :], 0.0).then_inc(two_left, 1)

            def turn(row, base, r, later):
                for n in range(len(row.chunks)):
                    if later and n == 3:
                        make_h1(r - 1, base, bass.ds((r - 1) % 2, 1))
                    if later and n == 6:
                        rest_of_z(r - 1)
                    if not later and n < 2:
                        rest_of_y(n)
                    if not later and n >= 5 and n % 2 == 1:
                        rest_of_y(n // 2)
                    for s in row.leaving_before(n):
                        take_out(s, row, base, r)
                    rest_of_chunk(n, base)

            turns(dve, turn)

            def window(w, parity, has):
                for n in range(len(closing)):
                    if n == 3 and has(0) and not has(1):
                        make_h1(blocks - 1, begins[phases], slice((blocks - 1) % 2, (blocks - 1) % 2 + 1))
                    if n == 0 and has(1) and not has(2):
                        rest_of_z(blocks - 1)
                    if n == 0 and has(4):
                        dve.wait_ge(rooted, w - 3)
                        if has(5):
                            dve.wait_ge(result_made, w - 4)
                        nc.vector.reciprocal(inverse[:, :], deviation[:, :]).then_inc(inverted, 1)
                        dve.wait_ge(inverted, w - 3)
                        nc.vector.scalar_tensor_tensor(out=shift[:, :], in0=mean_var[:, :, 0], scalar=-1.0,
                                                       in1=inverse[:, :], op0=ALU.mult, op1=ALU.mult)\
                            .then_inc(shift_made, 1)
                    if n == 1 and has(3):
                        dve.wait_ge(turned, w - 2)
                        for t in range(TILES):
                            last = nc.vector.bn_stats(stats[:, t, :], one[:, 1 - parity, t * D:(t + 1) * D])
                        last.then_inc(measured, 1)
                        dve.wait_ge(measured, w - 2)
                    if n == 3 and has(1):
                        dve.wait_ge(a_used, closing_base(w))
                        total = side[:, bass.ds(w - 1, 1), :]
                        nc.vector.tensor_tensor(total, again[:, 1 - parity:2 - parity, :], total, ALU.add)\
                            .then_inc(h2_summed, 1)
                    if has(0):
                        rest_of_chunk(n, closing_base(w))
                    if n == 1 and has(3):
                        for t in range(TILES):
                            last = nc.vector.bn_aggr(mean_var[:, t, :], stats[:, t, :])
                        last.then_inc(variance_made, 1)

            windows(dve, window)

        @block.gpsimd
        def _(pool):
            pool.wait_ge(z_summed, blocks)
            pool.wait_ge(weights_in, 64)

            def add_x(r, parity, first=False):
                if not first:
                    pool.wait_ge(turned, r)
                pool.wait_ge(h2_made, r + 1)
                pool.wait_ge(x_again_in[parity], r * 8 + (16 - 8 * parity))
                nc.gpsimd.tensor_tensor(row_t[:, None, :], side[:, bass.ds(r, 1), :], x_again[:, parity:parity + 1, :],
                                        ALU.add).then_inc(residual_made, 1)

            add_x(0, 0, True)
            add_x(1, 1)
            with pool.Fori(1, blocks // 2) as i:
                for parity in range(2):
                    add_x(i * 2 + parity, parity)

        @block.tensor
        def _(pe):
            def sum_chunk(n, base, targets, half, kb):
                slot = n % RING
                pe.wait_ge(a_lo_made, base + (n + 1))
                for t in range(HALF):
                    k = (HALF * half + t) * P
                    i = slice(t * BLOCK, (t + 1) * BLOCK)
                    for total, hi, lo, begins_here, ends_here in targets:
                        nc.tensor.matmul(total, lo[:, kb, k:k + P], a_hi[:, slot, i],
                                         start=begins_here and t == 0, stop=False)
                        nc.tensor.matmul(total, hi[:, kb, k:k + P], a_hi[:, slot, i], start=False, stop=False)
                        last = nc.tensor.matmul(total, hi[:, kb, k:k + P], a_lo[:, slot, i], start=False,
                                                stop=ends_here and t == HALF - 1)
                last.then_inc(a_used, 1)

            def sum_y(kb):
                if kb % X_GROUP == 0:
                    pe.wait_ge(x_in[kb // X_GROUP], 16)
                for t in range(TILES):
                    last = nc.tensor.matmul(small[:, kb % 2, t * D:(t + 1) * D], side[:, kb, t * P:(t + 1) * P],
                                            w1_sb[:, :], start=True, stop=True)
                last.then_inc(y_summed, 1)

            def sum_z(r):
                pe.wait_ge(weights_in, 64)
                pe.wait_ge(h1_made, r + 1)
                for t in range(TILES):
                    last = nc.tensor.matmul(small[:, 0, t * D:(t + 1) * D], row_t[:, t * P:(t + 1) * P],
                                            w2_sb[:, :], start=True, stop=True)
                last.then_inc(z_summed, 1)

            def turn(row, base, r, later):
                if not later:
                    pe.wait_ge(w1_in, 16)
                    sum_y(0)
                    sum_y(1)
                left = (r - row.start) * len(row.leaving) + (leaves[row.phase] + 1)
                parity = pe.snap(r % 2) if later else 0
                for n, (kind, q, kb, half) in enumerate(row.chunks):
                    targets = []
                    if kind in (LAYER1, FUSED):
                        if not later and half == 0:
                            pe.wait_ge(y_lo_made, kb + 1)
                        targets.append((one[:, bass.ds(parity, 1), :] if later else one[:, 0, :], y_hi, y_lo,
                                        n == row.first["one"], n == row.last["one"]))
                    if kind == FUSED:
                        if n == row.first["two"]:
                            pe.wait_ge(two_left, left)
                        targets.append((two[:, :], z_hi, z_lo, n == row.first["two"], n == row.last["two"]))
                    if kind == AGAIN:
                        if n == row.first[q]:
                            pe.wait_ge(two_left, left + (row.leaving.index(q - 2) + 1 if q >= 2 else 0))
                        targets.append((again[:, q % 2, :], z_hi, z_lo, n == row.first[q], n == row.last[q]))
                    if kind in (FUSED, AGAIN) and half == 0:
                        pe.wait_ge(z_lo_made, kb + 1)
                    sum_chunk(n, base, targets, half, kb)
                    if later and n == 1:
                        sum_z(r - 1)
                    if not later and half == CHUNKS - 1 and kb + 2 < blocks:
                        sum_y(kb + 2)

            turns(pe, turn)

            def window(w, parity, has):
                for n, (kb, half) in enumerate(closing):
                    if has(0):
                        if n == 0 and has(2):
                            pe.wait_ge(h2_summed, w - 1)
                        elif n == 0:
                            pe.wait_ge(two_left, leaves[phases] + 1)
                        if kb == blocks - 1 and half == 0 and not has(1):
                            pe.wait_ge(z_lo_made, blocks)
                        sum_chunk(n, closing_base(w), [(again[:, parity, :], z_hi, z_lo, n == 0, n == len(closing) - 1)],
                                  half, kb)
                        if n == 1 and not has(1):
                            sum_z(blocks - 1)
                    if n == 3 and has(2):
                        pe.wait_ge(residual_made, w - 1)
                        if has(4):
                            pe.wait_ge(result_made, w - 3)
                        for t in range(TILES):
                            last = nc.tensor.transpose(one[:, parity, t * D:(t + 1) * D],
                                                       row_t[:, t * P:(t + 1) * P], id_sb[:, :])
                        last.then_inc(turned, 1)

            windows(pe, window)


def kernel(x, adj, L0_gnn_W1, L0_gnn_b1, L0_gnn_W2, L0_gnn_b2):
    import numpy as np

    import concourse.bacc as bacc
    from concourse.bass_utils import run_bass_kernel_spmd

    n = adj.shape[0]
    blocks = n // BLOCK
    a_t = np.asarray(adj).reshape(blocks, BLOCK, blocks, CHUNKS, HALF, P).transpose(0, 2, 3, 5, 4, 1)
    arrays = {
        "a_t": np.ascontiguousarray(a_t).reshape(blocks * blocks * CHUNKS, P, HALF * BLOCK),
        "x_t": np.ascontiguousarray(np.asarray(x).T),
        "w1": np.asarray(L0_gnn_W1),
        "b1": np.asarray(L0_gnn_b1).reshape(D, 1),
        "w2": np.asarray(L0_gnn_W2),
        "b2": np.asarray(L0_gnn_b2).reshape(D, 1),
        "ident": np.eye(P, dtype=np.float32),
    }
    nc = bacc.Bacc("TRN2", target_bir_lowering=False, num_devices=1, dynamic_dma_scratch_size=2048)
    ins = [nc.dram_tensor(name, a.shape, F32, kind="ExternalInput").ap() for name, a in arrays.items()]
    out = nc.dram_tensor("out", (blocks, P, BLOCK), F32, kind="ExternalOutput").ap()
    gnn_kernel(nc, *ins, out)
    result = run_bass_kernel_spmd(nc, [arrays], core_ids=[0]).results[0]["out"]
    return np.asarray(result).reshape(blocks, P, TILES, D).transpose(0, 2, 1, 3).reshape(n, D)
```

```python
from contextlib import ExitStack

import concourse.bass as bass
from concourse import mybir

ALU = mybir.AluOpType
ACT = mybir.ActivationFunctionType
F32 = mybir.dt.float32
F32R = mybir.dt.float32r

P = 128
D = 128
BLOCK = 512
TILES = BLOCK // P
HALF = 2
CHUNKS = TILES // HALF
RING = 4
GROUP = 2
LAGS = 8
ALIGN = 32
ALONE = 2
EPS = 1e-5

LAYER1, FUSED, AGAIN = "layer1", "fused", "again"


def row_plan(phase, blocks):
    known = GROUP * phase
    own, ahead = list(range(known, known + GROUP)), list(range(known + GROUP, blocks))
    single = [(LAYER1, None, kb) for kb in (ahead[:-1] + own + ahead[-1:] if phase else own + ahead)]
    again = [(AGAIN, q, kb) for q in range(phase) for kb in range(known - GROUP, known)]
    fused = [(FUSED, None, kb) for kb in range(known)]
    begin = single[:-2][:2]
    light = begin + again + single[len(begin):-2]
    paired = len(light) - (ALONE if GROUP * (phase + 1) == blocks else 0)
    plan, used = [], 0
    for n, block in enumerate(light):
        plan.append(block)
        while used < min(len(fused), len(fused) * (n + 1) // paired):
            plan.append(fused[used])
            used += 1
    return plan + single[-2:]


def kept_column(j, c, blocks):
    return blocks - 2 * HALF * (c + 1) + j * HALF


def columns_kept(phase, blocks):
    return sum(GROUP * (phase + 1) <= kept_column(0, c, blocks) for c in range(GROUP))


class Row:

    def __init__(self, phase, blocks):
        self.phase, self.start = phase, GROUP * phase
        self.chunks = [(kind, q, kb, half) for kind, q, kb in row_plan(phase, blocks) for half in range(CHUNKS)]
        self.first, self.last = {}, {}
        for n, (kind, q, _, _) in enumerate(self.chunks):
            sums = {LAYER1: ["one"], FUSED: ["one", "two"], AGAIN: [q]}[kind]
            for s in sums:
                self.first.setdefault(s, n)
                self.last[s] = n
        self.leaving = sorted((s for s in self.last if s != "one"), key=lambda s: self.last[s])
        assert all(self.last[s] + RING < len(self.chunks) for s in self.leaving)
        assert len(self.chunks) % RING == 0
        self.last_of_column = {kb: n for n, (kind, _, kb, _) in enumerate(self.chunks) if kind == FUSED}
        self.keeps = {n: kb - self.start for n, (kind, _, kb, _) in enumerate(self.chunks)
                      if kind == LAYER1 and kb - self.start < columns_kept(phase, blocks)}
        self.rereads = {n: kb - self.start + GROUP for n, (kind, q, kb, _) in enumerate(self.chunks)
                        if kind == AGAIN and q == phase - 1
                        and kb - self.start + GROUP < columns_kept(phase - 1, blocks)}
        loaded = [n for n in range(len(self.chunks)) if n not in self.rereads]
        self.loads = [sum(m % RING == s for m in loaded) for s in range(RING)]
        self.loads_before = {n: sum(m % RING == n % RING for m in loaded if m < n) for n in loaded}
        self.load_after = {}
        for n in loaded:
            after = [m for m in loaded if m < n and m % RING == n % RING] or [n - RING]
            if n in self.keeps:
                after += [m for m, c in self.rereads.items() if c == self.keeps[n]
                          and self.chunks[m][3] == self.chunks[n][3]]
                assert max(after) < n
            self.load_after[n] = max(after)

    def leaving_before(self, n):
        return [s for s in self.leaving if self.last[s] + RING == n]

    def row_of(self, q, r):
        return r + (GROUP * q - self.start)


def gnn_kernel(nc, a_t, x_t, w1, b1, w2, b2, ident, out):
    blocks = x_t.shape[1] // BLOCK
    phases = blocks // GROUP
    rows = [Row(p, blocks) for p in range(phases)]
    per_row = [len(r.chunks) for r in rows]
    in_dram = blocks * CHUNKS
    begins = [GROUP * sum(per_row[:p]) for p in range(phases + 1)]
    leaves = [GROUP * sum(len(r.leaving) for r in rows[:p]) for p in range(phases + 1)]
    loads_begin = [[GROUP * sum(r.loads[s] for r in rows[:p]) for s in range(RING)] for p in range(phases + 1)]
    early = range(2 * GROUP, blocks - GROUP, 2)
    closing = [(kb, half) for kb in range(blocks - GROUP, blocks) for half in range(CHUNKS)]
    assert len(closing) == RING and blocks % 2 == 0 and GROUP == HALF == 2 and BLOCK == HALF * CHUNKS * P

    with ExitStack() as ctx:
        def sb(name, shape, dt=F32):
            return ctx.enter_context(nc.sbuf_tensor(name, shape, dt))

        def psum(name, shape):
            return ctx.enter_context(nc.psum_tensor(name, shape, F32))

        def sem(name):
            return ctx.enter_context(nc.semaphore(name))

        base_of_y = -(-nc.sbuf_base // ALIGN) * ALIGN
        y_hi = sb("y_hi", [P, blocks, BLOCK], F32R)
        y_lo = sb("y_lo", [P, blocks, BLOCK], F32R)
        z_hi = sb("z_hi", [P, blocks, BLOCK], F32R)
        z_lo = sb("z_lo", [P, blocks, BLOCK], F32R)
        size = blocks * BLOCK * mybir.dt.size(F32)
        y_place = [nc.alloc_sbuf_tensor_at(f"y_place{h}", [P, blocks, BLOCK], F32, offset=base_of_y + h * size)
                   for h in range(CHUNKS)]
        z_place = [nc.alloc_sbuf_tensor_at(f"z_place{h}", [P, blocks, BLOCK], F32, offset=base_of_y + (2 + h) * size)
                   for h in range(CHUNKS)]
        a_raw = sb("a_raw", [P, RING, HALF, BLOCK])
        a_hi = sb("a_hi", [P, RING, HALF, BLOCK], F32R)
        a_lo = sb("a_lo", [P, RING, HALF, BLOCK], F32R)
        side = sb("side", [P, blocks, BLOCK])
        row_t = sb("row_t", [P, 2, BLOCK])
        x_again = sb("x_again", [P, 2, BLOCK])
        result = sb("result", [P, 2, BLOCK])
        w1_sb = sb("w1_sb", [P, D])
        w2_sb = sb("w2_sb", [P, D])
        id_sb = sb("id_sb", [P, P])
        bias = sb("bias", [P, 2])
        stats = sb("stats", [P, TILES, 6])
        mean_var = sb("mean_var", [P, 2, TILES, 2])
        eps = sb("eps", [P, 1])
        guess = sb("guess", [P, TILES])
        newton = sb("newton", [P, TILES])
        inverse = sb("inverse", [P, TILES])
        shift = sb("shift", [P, TILES])

        one = psum("one", [P, 2, BLOCK])
        two = psum("two", [P, BLOCK])
        again = psum("again", [P, 2, BLOCK])
        small = psum("small", [P, 2, BLOCK])

        w1_in, weights_in, eps_set = sem("w1_in"), sem("weights_in"), sem("eps_set")
        x_in = [sem(f"x_in{g}") for g in range(blocks)]
        a_in = [sem(f"a_in{s}") for s in range(RING)]
        early_in = sem("early_in")
        second_in = [sem(f"second_in{h}") for h in range(CHUNKS)]
        kept_waits = sem("kept_waits")
        a_hi_made = sem("a_hi_made")
        a_lo_made = sem("a_lo_made")
        a_used = sem("a_used")
        y_summed, y_hi_made, y_lo_made = sem("y_summed"), sem("y_hi_made"), sem("y_lo_made")
        h1_made = sem("h1_made")
        z_summed, z_hi_made, z_lo_made = sem("z_summed"), sem("z_hi_made"), sem("z_lo_made")
        two_left = sem("two_left")
        h2_summed, h2_made = sem("h2_summed"), sem("h2_made")
        x_again_in = [sem(f"x_again_in{s}") for s in range(2)]
        residual_made, turned, measured = sem("residual_made"), sem("turned"), sem("measured")
        variance_made, rooted, inverted = sem("variance_made"), sem("rooted"), sem("inverted")
        shift_made, result_made = sem("shift_made"), sem("result_made")
        stored = [sem(f"stored{s}") for s in range(2)]

        def turns(eng, turn):
            for p, row in enumerate(rows):
                if p in (0, phases - 1):
                    for j in range(GROUP):
                        turn(row, j * per_row[p] + begins[p], j + row.start, p > 0 or j > 0)
                    continue
                with eng.Fori(0, GROUP) as j:
                    turn(row, j * per_row[p] + begins[p], j + row.start, True)

        def windows(eng, window):
            def at(w):
                window(w, w % 2, lambda lag: 0 <= w - lag < blocks)

            for w in range(LAGS):
                at(w)
            with eng.Fori(LAGS // 2, blocks // 2 - 1) as i:
                for parity in range(2):
                    window(i * 2 + parity, parity, lambda lag: True)
            for w in range(blocks - 2, blocks + LAGS):
                at(w)

        def closing_base(w):
            return w * len(closing) + begins[phases]

        def kept(j, c, half):
            return z_place[half][:, bass.ds(kept_column(j, c, blocks), HALF), :]

        def from_y(column, half):
            return y_place[half][:, bass.ds(column, HALF), :]

        def raw(n, row, r):
            _, _, kb, half = row.chunks[n]
            if n in row.keeps or n in row.rereads:
                return kept(r - row.start, row.keeps.get(n, row.rereads.get(n)), half)
            if row.phase == phases - 1 and r == blocks - 1 and kb >= blocks - GROUP:
                return from_y((kb - (blocks - GROUP)) * HALF, half)
            return a_raw[:, n % RING, :, :]

        def is_early(w, parity):
            return w in early if isinstance(w, int) else parity == 0

        def is_last(w):
            return isinstance(w, int) and w == blocks - 1

        def raw_closing(n, w, parity):
            kb, half = closing[n]
            if is_last(w):
                return from_y((kb - (blocks - GROUP)) * HALF, half)
            if is_early(w, parity):
                return from_y(w if kb == blocks - GROUP else blocks - HALF, half)
            return a_raw[:, n % RING, :, :]

        def others_before(w, parity):
            if isinstance(w, int):
                return w - sum(e < w for e in early)
            return (w - parity) // 2 + early[0] // 2

        def in_rows(w, lag, parity):
            banks = small if isinstance(w, int) and w - lag >= blocks - 2 else one
            return banks[:, (parity + lag) % 2, :]

        block = ctx.enter_context(nc.Block())

        @block.sync
        def _(sp):
            def load(n, place, chunk, after=None):
                if after is not None:
                    sp.wait_ge(a_lo_made, after)
                sp.dma_start(place, a_t[chunk, :, :, :]).then_inc(a_in[n % RING], 16)

            def load_x(kb):
                sp.dma_start(side[:, kb, :], x_t[:, kb * BLOCK:(kb + 1) * BLOCK]).then_inc(x_in[kb], 16)

            def turn(row, base, r, later):
                if not later:
                    sp.dma_start(w1_sb[:, :], w1).then_inc(w1_in, 16)
                    load_x(0)
                    load_x(1)
                last = row.phase == phases - 1 and r == blocks - 1
                for n, (kind, q, kb, half) in enumerate(row.chunks):
                    of = row.row_of(q, r) if kind == AGAIN else r
                    for w in early:
                        if last and n == min(row.last_of_column[w + 1] + 2 * RING, len(row.chunks) - 1):
                            sp.wait_ge(a_used, base + row.last_of_column[w + 1] + 1)
                            for h in range(CHUNKS):
                                sp.dma_start(from_y(w, h), a_t[w * in_dram + CHUNKS * (blocks - GROUP) + h, :, :, :])\
                                    .then_inc(early_in, 16)
                    if last and kind == LAYER1 and half == 0:
                        column = (kb - (blocks - GROUP)) * HALF + 1
                        sp.wait_ge(a_used, base + row.last_of_column[column] + 1)
                    if n not in row.rereads:
                        load(n, raw(n, row, r), of * in_dram + (CHUNKS * kb + half),
                             None if not later and n < RING else base + (row.load_after[n] + 1))
                    if not later and n == 0:
                        sp.dma_start(w2_sb[:, :], w2).then_inc(weights_in, 16)
                        sp.dma_start(bias[:, 0:1], b1).then_inc(weights_in, 16)
                        sp.dma_start(bias[:, 1:2], b2).then_inc(weights_in, 16)
                        sp.dma_start(id_sb[:, :], ident).then_inc(weights_in, 16)
                    if not later and half == 0 and kb + 2 < blocks:
                        load_x(kb + 2)

            turns(sp, turn)

            def window(w, parity, has):
                for n, (kb, half) in enumerate(closing):
                    chunk = w * in_dram + (CHUNKS * kb + half)
                    base = closing_base(w)
                    if n == (0 if isinstance(w, int) and w > early[-1] + 1 else 2) and has(7):
                        sp.wait_ge(result_made, w - 6)
                        sp.dma_start(out[w - 7, :, :], result[:, 1 - parity, :]).then_inc(stored[1 - parity], 16)
                    if not has(0) or is_last(w):
                        pass
                    elif is_early(w, parity):
                        if n == CHUNKS and isinstance(w, int) and w == early[0]:
                            sp.wait_ge(a_used, begins[phases])
                        if kb == blocks - 1:
                            if not isinstance(w, int) or w > early[0]:
                                sp.wait_ge(a_lo_made, base + (n + 1 - 2 * RING))
                            sp.dma_start(raw_closing(n, w, parity), a_t[chunk, :, :, :]).then_inc(second_in[half], 16)
                    else:
                        between = 2 if not isinstance(w, int) or w - 1 in early else 1
                        load(n, a_raw[:, n % RING, :, :], chunk, base + (n + 1 - between * RING))
                    if n == 0 and has(3):
                        if has(5):
                            sp.wait_ge(residual_made, w - 4)
                        sp.dma_start(x_again[:, 1 - parity, :], x_t[:, bass.ds((w - 3) * BLOCK, BLOCK)])\
                            .then_inc(x_again_in[1 - parity], 16)

            windows(sp, window)
            for parity in range(2):
                sp.wait_ge(stored[parity], 16 * (blocks // 2))

        @block.scalar
        def _(act):
            def round_chunk(n, base, place, loads, in_register=False, first=False):
                if loads is not None:
                    act.wait_ge(a_in[n % RING], loads)
                if not first:
                    act.wait_ge(a_used, base + (n - RING + 1))
                if in_register:
                    act.sem_inc(kept_waits, 1)
                nc.scalar.copy(a_hi[:, n % RING, :, :], place).then_inc(a_hi_made, 1)

            def round_y(kb):
                act.wait_ge(y_summed, kb + 1)
                nc.scalar.copy(y_hi[:, kb, :], small[:, kb % 2, :]).then_inc(y_hi_made, 1)

            def round_z(r):
                act.wait_ge(z_summed, r + 1)
                nc.scalar.copy(z_hi[:, bass.ds(r, 1), :], small[:, 0:1, :]).then_inc(z_hi_made, 1)

            def relu_h2(r):
                act.wait_ge(h2_summed, r + 1)
                h2_t = side[:, bass.ds(r, 1), :]
                nc.scalar.activation(h2_t, h2_t, ACT.Relu, bias=bias[:, 1:2]).then_inc(h2_made, 1)

            def normalise(w, parity, half):
                for t in range(TILES // 2 * half, TILES // 2 * (half + 1)):
                    cols = slice(t * D, (t + 1) * D)
                    scaled = nc.scalar.activation(result[:, 1 - parity, cols], in_rows(w, 5, parity)[:, cols],
                                                  ACT.Identity, scale=inverse[:, t:t + 1], bias=shift[:, t:t + 1])
                return scaled

            nc.scalar.preload_act_table(ACT.Sqrt)

            def turn(row, base, r, later):
                for n in range(len(row.chunks)):
                    if later and n == 6:
                        round_z(r - 1)
                    if not later and n < 2:
                        round_y(n)
                    if not later and n >= 5 and n % 2 == 1:
                        round_y(n // 2)
                    loads = None
                    if n not in row.rereads:
                        before = (r - row.start) * row.loads[n % RING] + loads_begin[row.phase][n % RING]
                        loads = before * 16 + 16 * (row.loads_before[n] + 1)
                    round_chunk(n, base, raw(n, row, r), loads, n in row.keeps and not isinstance(r, int),
                                not later and n < RING)

            turns(act, turn)

            def window(w, parity, has):
                for n in range(len(closing)):
                    if n == 0 and has(1) and not has(2):
                        round_z(blocks - 1)
                    if n == 0 and not has(0) and has(1):
                        relu_h2(w - 2)
                    if has(0):
                        loads = None
                        if is_last(w):
                            pass
                        elif is_early(w, parity):
                            if n == 0 and isinstance(w, int) and w == early[0]:
                                act.wait_ge(early_in, 16 * CHUNKS * len(early))
                            if n >= CHUNKS:
                                act.wait_ge(second_in[n - CHUNKS], w * 8 - (8 * early[0] - 16))
                        else:
                            loads = others_before(w, parity) * 16 + 16 * (loads_begin[phases][n] + 1)
                        round_chunk(n, closing_base(w), raw_closing(n, w, parity), loads)
                    if n == 0 and has(4):
                        if not has(5):
                            act.wait_ge(eps_set, 1)
                        act.wait_ge(variance_made, w - 3)
                        nc.scalar.activation(guess[:, :], mean_var[:, parity, :, 1], ACT.Sqrt, bias=eps[:, 0:1])\
                            .then_inc(rooted, 1)
                    if n == 0 and has(5):
                        act.wait_ge(shift_made, w - 4)
                        if has(7):
                            act.wait_ge(stored[1 - parity], w * 8 - (48 - 8 * parity))
                        normalise(w, parity, 0)
                    if n == 1 and has(5):
                        normalise(w, parity, 1).then_inc(result_made, 1)
                    if n == 2 and has(0) and has(2):
                        relu_h2(w - 2)
                    if n == 2 and not has(0) and has(1):
                        relu_h2(w - 1)

            windows(act, window)

        @block.vector
        def _(dve):
            def rest_of_chunk(n, base, place):
                dve.wait_ge(a_hi_made, base + (n + 1))
                nc.vector.tensor_tensor(a_lo[:, n % RING, :, :], place, a_hi[:, n % RING, :, :],
                                        ALU.subtract).then_inc(a_lo_made, 1)

            def rest_of_y(kb):
                dve.wait_ge(y_hi_made, kb + 1)
                nc.vector.tensor_tensor(y_lo[:, kb, :], small[:, kb % 2, :], y_hi[:, kb, :],
                                        ALU.subtract).then_inc(y_lo_made, 1)

            def rest_of_z(r):
                dve.wait_ge(z_hi_made, r + 1)
                nc.vector.tensor_tensor(z_lo[:, bass.ds(r, 1), :], small[:, 0:1, :], z_hi[:, bass.ds(r, 1), :],
                                        ALU.subtract).then_inc(z_lo_made, 1)

            def make_h1(r, chunks, parity):
                dve.wait_ge(weights_in, 64)
                dve.wait_ge(a_used, chunks)
                nc.vector.tensor_scalar(row_t[:, 0, :], one[:, parity, :], bias[:, 0:1], 0.0, ALU.add, ALU.max)\
                    .then_inc(h1_made, 1)

            def take_out(s, row, base, r):
                dve.wait_ge(a_used, base + (row.last[s] + 1))
                of = r if s == "two" else row.row_of(s, r)
                total = side[:, bass.ds(of, 1), :]
                part = two[:, None, :] if s == "two" else again[:, s % 2:s % 2 + 1, :]
                if s == "two" or row.phase == 1:
                    nc.vector.tensor_copy(total, part).then_inc(two_left, 1)
                else:
                    nc.vector.tensor_tensor(total, part, total, ALU.add).then_inc(two_left, 1)

            def add_sums(w, parity):
                dve.wait_ge(a_used, closing_base(w))
                total = side[:, bass.ds(w - 1, 1), :]
                nc.vector.tensor_tensor(total, again[:, 1 - parity:2 - parity, :], total, ALU.add)\
                    .then_inc(h2_summed, 1)

            nc.vector.memset(eps[:, :], EPS).then_inc(eps_set, 1)
            dve.wait_ge(eps_set, 1)
            nc.vector.memset(shift[:, :], 0.0).then_inc(two_left, 1)

            def turn(row, base, r, later):
                for n in range(len(row.chunks)):
                    if later and n == 3:
                        make_h1(r - 1, base, bass.ds((r - 1) % 2, 1))
                    if later and n == 6:
                        rest_of_z(r - 1)
                    if not later and n < 2:
                        rest_of_y(n)
                    if not later and n >= 5 and n % 2 == 1:
                        rest_of_y(n // 2)
                    for s in row.leaving_before(n):
                        take_out(s, row, base, r)
                    rest_of_chunk(n, base, raw(n, row, r))

            turns(dve, turn)

            def window(w, parity, has):
                for n in range(len(closing)):
                    if n == 3 and has(0) and not has(1):
                        make_h1(blocks - 1, begins[phases], slice((blocks - 1) % 2, (blocks - 1) % 2 + 1))
                    if n == 0 and has(1) and not has(2):
                        rest_of_z(blocks - 1)
                    if n == 1 and has(4):
                        dve.wait_ge(rooted, w - 3)
                        nc.vector.reciprocal(guess[:, :], guess[:, :]).then_inc(inverted, 1)
                    if n == 2 and has(4):
                        dve.wait_ge(inverted, w * 4 - 15)
                        nc.vector.scalar_tensor_tensor(out=newton[:, :], in0=mean_var[:, parity, :, 1], scalar=EPS,
                                                       in1=guess[:, :], op0=ALU.add, op1=ALU.mult)\
                            .then_inc(inverted, 1)
                    if n == 3 and has(4):
                        dve.wait_ge(inverted, w * 4 - 14)
                        nc.vector.scalar_tensor_tensor(out=newton[:, :], in0=newton[:, :], scalar=-0.5,
                                                       in1=guess[:, :], op0=ALU.mult, op1=ALU.mult)\
                            .then_inc(inverted, 1)
                    if n == 3 and not has(0) and has(1):
                        add_sums(w, parity)
                    if n == 3 and has(3):
                        dve.wait_ge(turned, w - 2)
                        for t in range(TILES):
                            last = nc.vector.bn_stats(stats[:, t, :], in_rows(w, 3, parity)[:, t * D:(t + 1) * D])
                        last.then_inc(measured, 1)
                    if n == 3 and has(0) and has(1):
                        add_sums(w, parity)
                    if n == 3 and has(3):
                        dve.wait_ge(measured, w - 2)
                    if n == 3 and has(4):
                        if has(5):
                            dve.wait_ge(result_made, w - 4)
                        dve.wait_ge(inverted, w * 4 - 13)
                        nc.vector.scalar_tensor_tensor(out=inverse[:, :], in0=newton[:, :], scalar=1.5,
                                                       in1=guess[:, :], op0=ALU.add, op1=ALU.mult)\
                            .then_inc(inverted, 1)
                    if n == 3 and has(3):
                        for t in range(TILES):
                            last = nc.vector.bn_aggr(mean_var[:, 1 - parity, t, :], stats[:, t, :])
                        last.then_inc(variance_made, 1)
                    if n == 3 and has(4):
                        dve.wait_ge(inverted, w * 4 - 12)
                        nc.vector.scalar_tensor_tensor(out=shift[:, :], in0=mean_var[:, parity, :, 0], scalar=-1.0,
                                                       in1=inverse[:, :], op0=ALU.mult, op1=ALU.mult)\
                            .then_inc(shift_made, 1)
                    if has(0):
                        rest_of_chunk(n, closing_base(w), raw_closing(n, w, parity))

            windows(dve, window)

        @block.gpsimd
        def _(pool):
            pool.wait_ge(z_summed, blocks)
            pool.wait_ge(weights_in, 64)

            def add_x(r, parity, first=False):
                if not first:
                    pool.wait_ge(turned, r - 1)
                pool.wait_ge(h2_made, r + 1)
                pool.wait_ge(x_again_in[parity], r * 8 + (16 - 8 * parity))
                nc.gpsimd.tensor_tensor(row_t[:, parity:parity + 1, :], side[:, bass.ds(r, 1), :],
                                        x_again[:, parity:parity + 1, :], ALU.add).then_inc(residual_made, 1)

            add_x(0, 0, True)
            add_x(1, 1, True)
            with pool.Fori(1, blocks // 2) as i:
                for parity in range(2):
                    add_x(i * 2 + parity, parity)

        @block.tensor
        def _(pe):
            def sum_chunk(n, base, targets, half, kb):
                slot = n % RING
                pe.wait_ge(a_lo_made, base + (n + 1))
                for t in range(HALF):
                    k = (HALF * half + t) * P
                    for total, hi, lo, begins_here, ends_here in targets:
                        nc.tensor.matmul(total, lo[:, kb, k:k + P], a_hi[:, slot, t, :],
                                         start=begins_here and t == 0, stop=False)
                        nc.tensor.matmul(total, hi[:, kb, k:k + P], a_hi[:, slot, t, :], start=False, stop=False)
                        last = nc.tensor.matmul(total, hi[:, kb, k:k + P], a_lo[:, slot, t, :], start=False,
                                                stop=ends_here and t == HALF - 1)
                last.then_inc(a_used, 1)

            def sum_y(kb):
                pe.wait_ge(x_in[kb], 16)
                for t in range(TILES):
                    last = nc.tensor.matmul(small[:, kb % 2, t * D:(t + 1) * D], side[:, kb, t * P:(t + 1) * P],
                                            w1_sb[:, :], start=True, stop=True)
                last.then_inc(y_summed, 1)

            def sum_z(r):
                pe.wait_ge(weights_in, 64)
                pe.wait_ge(h1_made, r + 1)
                for t in range(TILES):
                    last = nc.tensor.matmul(small[:, 0, t * D:(t + 1) * D], row_t[:, 0, t * P:(t + 1) * P],
                                            w2_sb[:, :], start=True, stop=True)
                last.then_inc(z_summed, 1)

            def turn(row, base, r, later):
                if not later:
                    pe.wait_ge(w1_in, 16)
                    sum_y(0)
                    sum_y(1)
                left = (r - row.start) * len(row.leaving) + (leaves[row.phase] + 1)
                parity = r % 2 if row.phase == 0 else pe.snap(r % 2)
                for n, (kind, q, kb, half) in enumerate(row.chunks):
                    targets = []
                    if kind in (LAYER1, FUSED):
                        if not later and half == 0:
                            pe.wait_ge(y_lo_made, kb + 1)
                        targets.append((one[:, bass.ds(parity, 1), :], y_hi, y_lo,
                                        n == row.first["one"], n == row.last["one"]))
                    if kind == FUSED:
                        if n == row.first["two"]:
                            pe.wait_ge(two_left, left)
                        targets.append((two[:, :], z_hi, z_lo, n == row.first["two"], n == row.last["two"]))
                    if kind == AGAIN:
                        if n == row.first[q]:
                            pe.wait_ge(two_left, left + (row.leaving.index(q - 2) + 1 if q >= 2 else 0))
                        targets.append((again[:, q % 2, :], z_hi, z_lo, n == row.first[q], n == row.last[q]))
                    if kind in (FUSED, AGAIN) and half == 0:
                        pe.wait_ge(z_lo_made, kb + 1)
                    sum_chunk(n, base, targets, half, kb)
                    if later and n == 1:
                        sum_z(r - 1)
                    if not later and half == CHUNKS - 1 and kb + 2 < blocks:
                        sum_y(kb + 2)

            turns(pe, turn)

            def window(w, parity, has):
                for n, (kb, half) in enumerate(closing):
                    if has(0):
                        if n == 0 and has(2):
                            pe.wait_ge(h2_summed, w - 1)
                        elif n == 0:
                            pe.wait_ge(two_left, leaves[phases] + 1)
                        if kb == blocks - 1 and half == 0 and not has(1):
                            pe.wait_ge(z_lo_made, blocks)
                        sum_chunk(n, closing_base(w), [(again[:, parity, :], z_hi, z_lo, n == 0, n == RING - 1)],
                                  half, kb)
                        if n == 1 and not has(1):
                            sum_z(blocks - 1)
                    if n == 0 and has(3):
                        pe.wait_ge(residual_made, w - 2)
                        if has(5) and not (isinstance(w, int) and w - 3 >= blocks - 2):
                            pe.wait_ge(result_made, w - 4)
                        for t in range(TILES):
                            last = nc.tensor.transpose(in_rows(w, 3, parity)[:, t * D:(t + 1) * D],
                                                       row_t[:, 1 - parity, t * P:(t + 1) * P], id_sb[:, :])
                        last.then_inc(turned, 1)

            windows(pe, window)


def kernel(x, adj, L0_gnn_W1, L0_gnn_b1, L0_gnn_W2, L0_gnn_b2):
    import numpy as np

    import concourse.bacc as bacc
    from concourse.bass_utils import run_bass_kernel_spmd

    n = adj.shape[0]
    blocks = n // BLOCK
    a_t = np.asarray(adj).reshape(blocks, BLOCK, blocks, CHUNKS, HALF, P).transpose(0, 2, 3, 5, 4, 1)
    arrays = {
        "a_t": np.ascontiguousarray(a_t).reshape(blocks * blocks * CHUNKS, P, HALF, BLOCK),
        "x_t": np.ascontiguousarray(np.asarray(x).T),
        "w1": np.asarray(L0_gnn_W1),
        "b1": np.asarray(L0_gnn_b1).reshape(D, 1),
        "w2": np.asarray(L0_gnn_W2),
        "b2": np.asarray(L0_gnn_b2).reshape(D, 1),
        "ident": np.eye(P, dtype=np.float32),
    }
    nc = bacc.Bacc("TRN2", target_bir_lowering=False, num_devices=1, dynamic_dma_scratch_size=2048)
    ins = [nc.dram_tensor(name, a.shape, F32, kind="ExternalInput").ap() for name, a in arrays.items()]
    out = nc.dram_tensor("out", (blocks, P, BLOCK), F32, kind="ExternalOutput").ap()
    gnn_kernel(nc, *ins, out)
    result = run_bass_kernel_spmd(nc, [arrays], core_ids=[0]).results[0]["out"]
    return np.asarray(result).reshape(blocks, P, TILES, D).transpose(0, 2, 1, 3).reshape(n, D)
```
